# Optimizing a Trainium2 kernel written in Bass

```python
import numpy as np
import jax
import jax.numpy as jnp

def _softmax(x, axis=-1):
    return jax.nn.softmax(x, axis=axis)

def _gelu(x):
    return jax.nn.gelu(x, approximate=True)

def _silu(x):
    return jax.nn.silu(x)

def _sigmoid(x):
    return jax.nn.sigmoid(x)

def _layernorm(x, axis=-1, eps=1e-05):
    m = jnp.mean(x, axis=axis, keepdims=True)
    v = jnp.var(x, axis=axis, keepdims=True)
    return (x - m) / jnp.sqrt(v + eps)

def _scatter_add(tgt, idx, src, axis=0):
    return tgt.at[idx].add(src)

def _segment_sum(src, seg, n):
    return jax.ops.segment_sum(src, seg, n)
kernel_name = 'mk_adaln_ffn_d1_seqx_r8_cf108a'

def setup_inputs(seed: int=0):
    np.random.seed(seed)
    _w = jnp.asarray

    def _rec_inputs():
        import jax
        import jax.numpy as jnp
        _rk = jax.random.key(seed)
        x = 8.748e-05 + 1 * jax.random.normal(jax.random.fold_in(_rk, 1), (16, 128, 256), jnp.float32)
        _lenS = 128 - jax.random.randint(jax.random.fold_in(_rk, 7), (16,), 0, max(1, 128 // 4) + 1, jnp.int32)
        _lenS2 = 128 - jax.random.randint(jax.random.fold_in(_rk, 8), (16,), 0, max(1, 128 // 4) + 1, jnp.int32)
        cond_2048 = -9.80646e-05 + 1.00041 * jax.random.normal(jax.random.fold_in(_rk, 11), (16, 256), jnp.float32)
        return (x, cond_2048)
    x, cond_2048 = _rec_inputs()

    def _L0_cond_setup():
        import jax, jax.numpy as jnp
        import numpy as np
        DT = 0.01
        EPSILON = 0.08
        ALPHA = 0.7
        BETA = 0.8
        CLAMP = 20.0
        B, T, N = (32, 128, 256)

        def _derivative(q, p, drive, coupling, bias):
            i_couple = jnp.tanh(q) @ coupling.T
            dq = q - q ** 3 / 3.0 - p + drive + i_couple + bias
            dp = EPSILON * (q + ALPHA - BETA * p)
            return (dq, dp)

        def _rk4_step(q, p, drive, coupling, bias):
            dq1, dp1 = _derivative(q, p, drive, coupling, bias)
            dq2, dp2 = _derivative(q + 0.5 * DT * dq1, p + 0.5 * DT * dp1, drive, coupling, bias)
            dq3, dp3 = _derivative(q + 0.5 * DT * dq2, p + 0.5 * DT * dp2, drive, coupling, bias)
            dq4, dp4 = _derivative(q + DT * dq3, p + DT * dp3, drive, coupling, bias)
            q_next = q + DT / 6.0 * (dq1 + 2 * dq2 + 2 * dq3 + dq4)
            p_next = p + DT / 6.0 * (dp1 + 2 * dp2 + 2 * dp3 + dp4)
            q_next = jnp.clip(q_next, -CLAMP, CLAMP)
            p_next = jnp.clip(p_next, -CLAMP, CLAMP)
            return (q_next, p_next)
        key = jax.random.key(seed)
        k1, k2, k3, k4 = jax.random.split(key, 4)
        return {'q0': jax.random.normal(k1, (B, N), dtype=jnp.float32), 'p0': jax.random.normal(k2, (B, N), dtype=jnp.float32), 'input_drive_seq': jax.random.normal(k3, (B, T, N), dtype=jnp.float32), 'coupling': jax.random.normal(k4, (N, N), dtype=jnp.float32) * 0.01, 'bias': jnp.zeros((N,), dtype=jnp.float32)}
    _L0_cond_all = _L0_cond_setup()
    _L0_cond_in = {k: v for k, v in _L0_cond_all.items() if k in ('coupling', 'bias')}
    del _L0_cond_all

    def _L0_ffn_setup():
        import jax, jax.numpy as jnp
        import numpy as np
        H = 256
        I_MOE = 176
        I_SH = 704
        E = 8
        TOP_K = 2
        B, S = (1, 256)

        def _silu_and_mul(gu, inter):
            return jax.nn.silu(gu[..., :inter]) * gu[..., inter:]
        key = jax.random.key(seed)
        ks = jax.random.split(key, 7)
        sc = 0.02
        return {'hidden_states': jax.random.normal(ks[0], (B, S, H), jnp.float32), 'W_router': jax.random.normal(ks[1], (E, H), jnp.float32) * sc, 'W_sgate': jax.random.normal(ks[2], (1, H), jnp.float32) * sc, 'Ws_gate_up': jax.random.normal(ks[3], (H, 2 * I_SH), jnp.float32) * sc, 'Ws_down': jax.random.normal(ks[4], (I_SH, H), jnp.float32) * sc, 'We_gate_up': jax.random.normal(ks[5], (E, H, 2 * I_MOE), jnp.float32) * sc, 'We_down': jax.random.normal(ks[6], (E, I_MOE, H), jnp.float32) * sc}
    _L0_ffn_all = _L0_ffn_setup()
    _L0_ffn_in = {k: v for k, v in _L0_ffn_all.items() if k in ('W_router', 'W_sgate', 'Ws_gate_up', 'Ws_down', 'We_gate_up', 'We_down')}
    del _L0_ffn_all
    return {'x': x, 'cond_2048': cond_2048, 'L0_cond_coupling': _L0_cond_in['coupling'], 'L0_cond_bias': _L0_cond_in['bias'], 'L0_ffn_W_router': _L0_ffn_in['W_router'], 'L0_ffn_W_sgate': _L0_ffn_in['W_sgate'], 'L0_ffn_Ws_gate_up': _L0_ffn_in['Ws_gate_up'], 'L0_ffn_Ws_down': _L0_ffn_in['Ws_down'], 'L0_ffn_We_gate_up': _L0_ffn_in['We_gate_up'], 'L0_ffn_We_down': _L0_ffn_in['We_down']}

def reference(x, cond_2048, L0_cond_coupling, L0_cond_bias, L0_ffn_W_router, L0_ffn_W_sgate, L0_ffn_Ws_gate_up, L0_ffn_Ws_down, L0_ffn_We_gate_up, L0_ffn_We_down):
    import jax
    import jax.numpy as jnp

    def _L0_cond_ref(q0, p0, input_drive_seq, coupling, bias):
        import jax, jax.numpy as jnp
        import numpy as np
        DT = 0.01
        EPSILON = 0.08
        ALPHA = 0.7
        BETA = 0.8
        CLAMP = 20.0
        B, T, N = (32, 128, 256)

        def _derivative(q, p, drive, coupling, bias):
            i_couple = jnp.tanh(q) @ coupling.T
            dq = q - q ** 3 / 3.0 - p + drive + i_couple + bias
            dp = EPSILON * (q + ALPHA - BETA * p)
            return (dq, dp)

        def _rk4_step(q, p, drive, coupling, bias):
            dq1, dp1 = _derivative(q, p, drive, coupling, bias)
            dq2, dp2 = _derivative(q + 0.5 * DT * dq1, p + 0.5 * DT * dp1, drive, coupling, bias)
            dq3, dp3 = _derivative(q + 0.5 * DT * dq2, p + 0.5 * DT * dp2, drive, coupling, bias)
            dq4, dp4 = _derivative(q + DT * dq3, p + DT * dp3, drive, coupling, bias)
            q_next = q + DT / 6.0 * (dq1 + 2 * dq2 + 2 * dq3 + dq4)
            p_next = p + DT / 6.0 * (dp1 + 2 * dp2 + 2 * dp3 + dp4)
            q_next = jnp.clip(q_next, -CLAMP, CLAMP)
            p_next = jnp.clip(p_next, -CLAMP, CLAMP)
            return (q_next, p_next)
        drive_tbn = jnp.swapaxes(input_drive_seq, 0, 1)

        def scan_fn(carry, drive):
            q, p = carry
            q, p = _rk4_step(q, p, drive, coupling, bias)
            return ((q, p), q)
        (_, _), q_trace_tbn = jax.lax.scan(scan_fn, (q0, p0), drive_tbn)
        return jnp.swapaxes(q_trace_tbn, 0, 1)

    def _L0_ffn_ref(hidden_states, W_router, W_sgate, Ws_gate_up, Ws_down, We_gate_up, We_down):
        import jax, jax.numpy as jnp
        import numpy as np
        H = 256
        I_MOE = 176
        I_SH = 704
        E = 8
        TOP_K = 2
        B, S = (1, 256)

        def _silu_and_mul(gu, inter):
            return jax.nn.silu(gu[..., :inter]) * gu[..., inter:]
        orig_shape = hidden_states.shape
        x = hidden_states.reshape(-1, H)
        T = x.shape[0]
        logits = x @ W_router.T
        probs = jax.nn.softmax(logits.astype(jnp.float32), axis=-1)
        rw, sel = jax.lax.top_k(probs, TOP_K)
        rw = rw.astype(x.dtype)
        combine = jnp.zeros((T, E), x.dtype).at[jnp.arange(T)[:, None], sel].add(rw)
        sh = _silu_and_mul(x @ Ws_gate_up, I_SH) @ Ws_down
        shared_out = sh * jax.nn.sigmoid(x @ W_sgate.T)
        gu = jnp.einsum('th,ehi->eti', x, We_gate_up)
        h = _silu_and_mul(gu, I_MOE)
        eo = jnp.einsum('eti,eih->eth', h, We_down)
        sparse_out = jnp.einsum('eth,te->th', eo, combine)
        return (shared_out + sparse_out).reshape(orig_shape)
    x = x + _L0_ffn_ref(_L0_cond_ref(cond_2048, cond_2048, x, L0_cond_coupling, L0_cond_bias), L0_ffn_W_router, L0_ffn_W_sgate, L0_ffn_Ws_gate_up, L0_ffn_Ws_down, L0_ffn_We_gate_up, L0_ffn_We_down)
    return x

_drawn_inputs = setup_inputs


def setup_inputs(seed=0):
    import zlib

    import numpy as np

    out = dict(_drawn_inputs(seed))
    spreads = {'L0_cond_bias': (0.0, 0.8)}
    factors = {'cond_2048': 7.696,
     'L0_cond_coupling': 8.0,
     'L0_ffn_W_router': 8.0,
     'L0_ffn_W_sgate': 8.0,
     'L0_ffn_Ws_gate_up': 7.813,
     'L0_ffn_Ws_down': 7.985,
     'L0_ffn_We_gate_up': 8.0,
     'L0_ffn_We_down': 8.0}
    for name, (base, spread) in spreads.items():
        noise = np.random.default_rng([zlib.crc32(name.encode()), seed]).standard_normal(out[name].shape)
        drawn = base * np.exp(spread * noise) if base else spread * noise
        out[name] = jnp.asarray(drawn.astype(out[name].dtype))
    for name, factor in factors.items():
        out[name] = (out[name] * factor).astype(out[name].dtype)
    return out
```

```python
from contextlib import ExitStack

import concourse.bass as bass
from concourse import mybir

F32 = mybir.dt.float32
F16 = mybir.dt.float16
BF16 = mybir.dt.bfloat16
U32 = mybir.dt.uint32
ALU = mybir.AluOpType
ACT = mybir.ActivationFunctionType
AX = mybir.AxisListType

P = 128
B, T, N = 16, 128, 256
KC = N // P
CB = KC * B
STEPS = 8
BLOCKS = T // STEPS
TOK = STEPS * B
STAGES = 4 * STEPS
E, I_MOE, I_SH = 8, 176, 704
F = E * I_MOE + I_SH
TILES = -(-F // P)
FP = TILES * P
GROUP = 4
GROUPS = -(-TILES // GROUP)

DT, EPSILON, ALPHA, BETA, CLAMP = 0.01, 0.08, 0.7, 0.8, 20.0
C = [0.5 * DT, 0.5 * DT, DT, DT / 6.0]
SHIFT = ALPHA / BETA
A = [c * EPSILON for c in C]
W3 = 11184811 / 2.0 ** 25
W1 = 1.0 - 2.0 * W3

UP_AT = [1, 3, 4, 6, 8, 9, 11, 12, 13, 14, 17, 20, 21, 24, 25, 28, 29]
SPREAD_AT = [12, 15, 18, 21, 26]
DOWN_AT = [14, 15, 16, 17, 19, 22, 22, 23, 23, 26, 26, 27, 29, 30, 30, 31, 31]
SILU_AT = [s + 1 for s in UP_AT]
COPY_AT = [SPREAD_AT[j // GROUP] + 1 + (j % GROUP) // 2 for j in range(TILES)]
WEIGH_AT = [13, 14, 14, 15, 16, 16, 17, 18, 19, 20, 20, 22, 23, 26, 26, 29, 30]
assert len(UP_AT) == len(DOWN_AT) == len(WEIGH_AT) == TILES and len(SPREAD_AT) == GROUPS
assert all(w >= max(s, c) and d > w for w, s, c, d in zip(WEIGH_AT, SILU_AT, COPY_AT, DOWN_AT))
WARM = [2, 6, 6, 6, 6, 6, 6, 6, 6, 6, 6, 6, 0, 6, 6, 6, 6, 0, 4, 6, 6, 0, 6, 4, 0, 6, 0, 8, 6, 6, 2, 0]
DRIVES = (C[0], C[2], C[3])
ROUTE_OPS = 7
FINISH_AT = [2, 4]


def program(nc, x, cond, coupling, bias, w_up, w_down, w_route, identity, spread, iota, e_base, out):
    ctx = ExitStack()
    with ctx:
        def sb(name, shape, dt=F32):
            return ctx.enter_context(nc.sbuf_tensor(name, shape, dt))

        def pb(name):
            return ctx.enter_context(nc.psum_tensor(name, [P, 512], F32))

        def sem(name):
            return ctx.enter_context(nc.semaphore(name))

        xs = sb("xs", [P, T, KC, B])
        cf = sb("cf", [P, KC, N])
        bias_s = sb("bias_s", [P, KC])
        wf = sb("wf", [P, KC, 2, F])
        wd = sb("wd", [P, TILES, N])
        wr = sb("wr", [P, KC, E + 1])
        ident = sb("ident", [P, P])
        ident_b = sb("ident_b", [P, P], BF16)
        sel = sb("sel", [96, FP], BF16)
        iota_s = sb("iota_s", [P, E])
        e_s = sb("e_s", [P, E])
        ones = sb("ones", [P, P])
        c16 = sb("c16", [P, 2, KC, N], F16)
        w16 = sb("w16", [P, 2, KC, 2, FP], F16)
        drive = sb("drive", [P, T + 1, 3, KC, B])
        bias_c = sb("bias_c", [P, 3, KC])
        most = sb("most", [P, 2])
        most1 = sb("most1", [1, 2])
        ebits = sb("ebits", [P, 2], U32)
        scale = sb("scale", [P, 2])
        unscale = sb("unscale", [P, 2])
        c_un = sb("c_un", [P, 4])
        q_trace = sb("q_trace", [P, KC, STEPS, B])
        q_raw = sb("q_raw", [P, KC, B])
        q_in = [None] + [sb(f"q{k}", [P, KC, B]) for k in (2, 3, 4)]
        p_in = [sb(f"p{k}", [P, KC, B]) for k in (1, 2, 3, 4)]
        p_raw = sb("p_raw", [P, KC, B])
        th_hi = sb("th_hi", [P, KC, B], F16)
        th_lo = sb("th_lo", [P, KC, B], F16)
        th = sb("th", [P, KC, B])
        square = sb("square", [P, KC, B])
        cubic = sb("cubic", [P, KC, B])
        force = sb("force", [P, KC, B])
        slope = sb("slope", [P, KC, B])
        rest = sb("rest", [P, KC, B])
        rest4 = sb("rest4", [P, KC, B])
        s2 = sb("s2", [P, KC, B])
        s3 = sb("s3", [P, KC, B])
        s4 = sb("s4", [P, KC, B])
        drive_now = sb("drive_now", [P, 3, KC, B])
        dqd = sb("dqd", [P, KC, B])
        w3_t = sb("w3_t", [P, KC, B])
        w1_t = sb("w1_t", [P, KC, B])
        dq = sb("dq", [P, KC, B])
        dq3 = sb("dq3", [P, KC, B])
        dp = sb("dp", [P, KC, B])
        dp3 = sb("dp3", [P, KC, B])
        pw3 = sb("pw3", [P, KC, B])
        pv3 = sb("pv3", [P, KC, B])
        pw4 = sb("pw4", [P, KC, B])
        pv4 = sb("pv4", [P, KC, B])
        q_hi = sb("q_hi", [P, KC, TOK], F16)
        q_lo = sb("q_lo", [P, KC, TOK], F16)
        logit = sb("logit", [P, E + 1])
        top = sb("top", [P, 1])
        shifted = sb("shifted", [P, E])
        expo = sb("expo", [P, E])
        best = sb("best", [P, 8])
        which = sb("which", [P, 8], U32)
        which_f = sb("which_f", [P, 2])
        total = sb("total", [P, 1])
        share = sb("share", [P, 1])
        prob = sb("prob", [P, 2])
        first = sb("first", [P, E])
        second = sb("second", [P, E])
        gate_t = sb("gate_t", [P, 1])
        comb = sb("comb", [P, E + 1])
        comb_r = sb("comb_r", [P, E + 1])
        comb3 = sb("comb3", [P, 3, 32], BF16)
        comb_t = sb("comb_t", [96, TOK], BF16)
        comb_s = sb("comb_s", [P, TILES, TOK])
        act_s = sb("act_s", [P, 4, TOK])
        hidden = sb("hidden", [P, TILES, TOK])
        out_s = sb("out_s", [P, KC, TOK])

        coup_ps = pb("coup_ps")
        route_ps = pb("route_ps")
        up_ps = [pb(f"up_ps{i}") for i in range(4)]
        down_ps = pb("down_ps")
        warm_ps = pb("warm_ps")
        comb_tp = route_ps[0:96, 64:128].bitcast(BF16)

        in_core = sem("in_core")
        in_const = sem("in_const")
        in_x = sem("in_x")
        in_w = sem("in_w")
        in_wd = sem("in_wd")
        setup_v = sem("setup_v")
        setup_t = sem("setup_t")
        setup_a = sem("setup_a")
        zeroed = sem("zeroed")

        q_ready = sem("q_ready")
        hi_ready = sem("hi_ready")
        tanh_ready = sem("tanh_ready")
        lo_ready = sem("lo_ready")
        coupled = sem("coupled")
        squared = sem("squared")
        cubed = sem("cubed")
        forced = sem("forced")
        sloped = sem("sloped")
        p_ready = sem("p_ready")
        rested = sem("rested")
        q_clipped = sem("q_clipped")
        p_clipped = sem("p_clipped")
        parted = sem("parted")
        s4_ready = sem("s4_ready")
        drive_at = sem("drive_at")
        base_ready = sem("base_ready")

        q_split = sem("q_split")
        logits_ready = sem("logits_ready")
        routed = sem("routed")
        exp_ready = sem("exp_ready")
        gate_ready = sem("gate_ready")
        prob_ready = sem("prob_ready")
        turned = sem("turned")
        turned_copied = sem("turned_copied")
        spread_ready = sem("spread_ready")
        comb_copied = sem("comb_copied")
        up_ready = sem("up_ready")
        silu_ready = sem("silu_ready")
        hidden_ready = sem("hidden_ready")
        weighed = sem("weighed")
        down_ready = sem("down_ready")
        out_ready = sem("out_ready")
        stored = sem("stored")

        SETUP_V = 21
        PARTS = 6
        (B_S2, B_S3, B_DP, B_DQ, B_DQ3, B_DQD, B_DP3, B_PW3, B_PV3, B_PW4, B_PV4, B_NOW) = range(1, 13)
        BASE = B_NOW

        block = ctx.enter_context(nc.Block())

        def q0_of(i):
            return q_trace[:, :, (i - 1) % STEPS, :]

        def blocks(eng, block_of):
            block_of(0, None, False)
            block_of(1, 0, False)
            with eng.Fori(2, BLOCKS) as b:
                block_of(b, b - 1, True)

        @block.sync
        def _(sync):
            sync.dma_start(cf[:], coupling).then_inc(in_core, 16)
            sync.dma_start(q_trace[:, :, STEPS - 1, :], cond).then_inc(in_core, 16)
            sync.dma_start(q_raw[:], cond).then_inc(in_core, 16)
            sync.dma_start(p_raw[:], cond).then_inc(in_core, 16)
            sync.dma_start(bias_s[:], bias).then_inc(in_core, 16)
            sync.dma_start(ident[:], identity).then_inc(in_const, 16)
            sync.dma_start(xs[:], x).then_inc(in_x, 16)
            sync.dma_start(wf[:], w_up).then_inc(in_w, 16)
            sync.dma_start(wr[:], w_route).then_inc(in_const, 16)
            sync.dma_start(sel[:], spread).then_inc(in_const, 16)
            sync.dma_start(iota_s[:], iota).then_inc(in_const, 16)
            sync.dma_start(e_s[:], e_base).then_inc(in_const, 16)
            sync.dma_start(wd[:, 0:TILES - 1, :], w_down[0:(TILES - 1) * P, :].rearrange(
                "(j p) n -> p j n", p=P)).then_inc(in_wd, 16)
            sync.dma_start(wd[0:F % P, TILES - 1, :], w_down[(TILES - 1) * P:F, :]).then_inc(in_wd, 16)

            def store(f):
                sync.wait_ge(out_ready, KC * (f + 1))
                sync.dma_start(out[:, :, bass.ts(f, TOK)], out_s[:]).then_inc(stored, 16)

            with sync.Fori(0, BLOCKS) as f:
                store(f)
            sync.wait_ge(stored, 16 * BLOCKS)

        @block.scalar
        def _(act):
            act.wait_ge(zeroed, 1)
            nc.scalar.activation(gate_t[:], gate_t[:], ACT.Silu)
            act.wait_ge(in_core, 5 * 16)
            for d, c in enumerate(DRIVES):
                nc.scalar.activation(bias_c[:, d, :], bias_s[:], ACT.Copy, bias=-c * SHIFT, scale=c
                                     ).then_inc(setup_a, 1)
            act.wait_ge(setup_a, 3)
            act.wait_ge(in_x, 16)
            for m in range(KC):
                for d, c in enumerate(DRIVES):
                    nc.scalar.activation(drive[:, 0:T, d, m, :], xs[:, :, m, :], ACT.Identity,
                                         bias=bias_c[:, d, m:m + 1], scale=c).then_inc(setup_a, 1)

            def tanh(b, st):
                if st % 4:
                    q = q_in[st % 4]
                else:
                    q = q_raw
                if isinstance(b, int) and b == 0 and st == 0:
                    act.wait_ge(in_core, 5 * 16)
                else:
                    act.wait_ge(q_ready, b * STAGES + st)
                nc.scalar.activation(th_hi[:], q[:], ACT.Tanh).then_inc(hi_ready, 1)
                nc.scalar.activation(th[:], q[:], ACT.Tanh).then_inc(tanh_ready, 1)

            def ffn(f, st):
                if st == 0:
                    act.wait_ge(q_clipped, (f + 1) * STEPS)
                    if not (isinstance(f, int) and f == 0):
                        act.wait_ge(up_ready, f * TILES)
                    nc.scalar.copy(q_hi[:], q_trace[:].rearrange("p m t b -> p m (t b)")).then_inc(q_split, 1)
                if st == 2:
                    act.wait_ge(routed, f * ROUTE_OPS + 1)
                    nc.scalar.activation(gate_t[:], logit[:, E:E + 1], ACT.Tanh, scale=0.5).then_inc(gate_ready, 1)
                if st == 5:
                    act.wait_ge(routed, f * ROUTE_OPS + 5)
                    nc.scalar.mul(prob[:], best[:, 0:2], share[:, 0:1]).then_inc(prob_ready, 1)
                if st in (8, 9):
                    act.wait_ge(parted, f * PARTS + (2, 4)[st - 8])
                    if st == 8:
                        nc.scalar.copy(comb3[:, 0, 0:E + 1], comb[:]).then_inc(parted, 1)
                    else:
                        nc.scalar.copy(comb3[:, 1, 0:E + 1], comb_r[:]).then_inc(parted, 1)
                if st == SPREAD_AT[0] - 1:
                    act.wait_ge(turned, f + 1)
                    nc.scalar.copy(comb_t[:], comb_tp).then_inc(turned_copied, 1)
                for j in range(TILES):
                    if SILU_AT[j] == st:
                        act.wait_ge(up_ready, f * TILES + j + 1)
                        if not (isinstance(f, int) and f * TILES + j < 4):
                            act.wait_ge(hidden_ready, f * TILES + j - 3)
                        nc.scalar.activation(act_s[:, j % 4, :], up_ps[j % 4][:, 0:TOK], ACT.Silu,
                                             scale=unscale[:, 1:2]).then_inc(silu_ready, 1)
                    if COPY_AT[j] == st:
                        act.wait_ge(spread_ready, f * GROUPS + j // GROUP + 1)
                        if not (isinstance(f, int) and f == 0):
                            act.wait_ge(weighed, f * TILES + j - TILES + 1)
                        nc.scalar.copy(comb_s[:, j, :], route_ps[:, (j % GROUP) * TOK:(j % GROUP + 1) * TOK]
                                       ).then_inc(comb_copied, 1)

            def one_block(b, f, finish):
                for st in range(STAGES):
                    tanh(b, st)
                    if f is not None:
                        if isinstance(f, int) and st == 0:
                            act.wait_ge(setup_v, SETUP_V)
                        ffn(f, st)

            blocks(act, one_block)
            for st in range(STAGES):
                ffn(BLOCKS - 1, st)

        @block.tensor
        def _(pe):
            def largest(n, col):
                pe.wait_ge(setup_v, n)
                nc.tensor.matmul(route_ps[0:1, 0:P], most[:, col:col + 1], ident[:], start=True,
                                 stop=True).then_inc(setup_t, 1)
                pe.wait_ge(setup_v, n + 1)
                nc.tensor.matmul(route_ps[:, 0:1], ones[0:1, :], most1[0:1, col:col + 1], start=True,
                                 stop=True).then_inc(setup_t, 1)

            pe.wait_ge(in_const, 5 * 16)
            largest(1, 0)
            largest(10, 1)

            def couple(b, st):
                pe.wait_ge(hi_ready, b * STAGES + st + 1)
                if isinstance(b, int) and b == 0 and st == 0:
                    pe.wait_ge(setup_v, 9)
                for part in range(2):
                    for m in range(KC):
                        for k in range(KC):
                            nc.tensor.matmul(coup_ps[:, m * B:(m + 1) * B], c16[:, part, k, m * P:(m + 1) * P],
                                             th_hi[:, k, :], start=part == m == k == 0, stop=False,
                                             skip_group_check=True)
                pe.wait_ge(lo_ready, b * STAGES + st + 1)
                for m in range(KC):
                    for k in range(KC):
                        last = nc.tensor.matmul(coup_ps[:, m * B:(m + 1) * B], c16[:, 0, k, m * P:(m + 1) * P],
                                                th_lo[:, k, :], start=False, stop=True, skip_group_check=True)
                last.then_inc(coupled, 1)

            def ffn(f, st):
                first_block = isinstance(f, int) and f == 0
                if st == 0:
                    pe.wait_ge(q_clipped, (f + 1) * STEPS)
                    if not first_block:
                        pe.wait_ge(comb_copied, f * TILES)
                    for k in range(KC):
                        last = nc.tensor.matmul(route_ps[:, 0:E + 1], q_trace[:, k, :, :], wr[:, k, :],
                                                start=k == 0, stop=k == KC - 1)
                    last.then_inc(logits_ready, 1)
                if st == SPREAD_AT[0] - 2:
                    pe.wait_ge(parted, (f + 1) * PARTS)
                    nc.tensor.transpose(comb_tp, comb3[:].rearrange("p a b -> p (a b)"), ident_b[:]
                                        ).then_inc(turned, 1)
                for g in range(GROUPS):
                    if SPREAD_AT[g] == st:
                        if g == 0:
                            pe.wait_ge(turned_copied, f + 1)
                        else:
                            pe.wait_ge(comb_copied, f * TILES + g * GROUP)
                        tiles = range(g * GROUP, min(TILES, (g + 1) * GROUP))
                        for j in tiles:
                            last = nc.tensor.matmul(route_ps[:, (j % GROUP) * TOK:(j % GROUP + 1) * TOK],
                                                    sel[:, j * P:(j + 1) * P], comb_t[:], start=True, stop=True)
                        last.then_inc(spread_ready, 1)
                for j in range(TILES):
                    if UP_AT[j] == st:
                        if j == 0:
                            pe.wait_ge(q_split, 2 * (f + 1))
                        if not (isinstance(f, int) and f * TILES + j < 4):
                            pe.wait_ge(hidden_ready, f * TILES + j - 3)
                        for h in range(2):
                            n = 0
                            for k in range(KC):
                                for part, q in ((0, q_hi), (0, q_lo), (1, q_hi)):
                                    last = nc.tensor.matmul(
                                        up_ps[j % 4][:, h * TOK:(h + 1) * TOK],
                                        w16[:, part, k, h, j * P:(j + 1) * P], q[:, k, :],
                                        start=n == 0, stop=n == 3 * KC - 1)
                                    n += 1
                        last.then_inc(up_ready, 1)
                for j in range(TILES):
                    if DOWN_AT[j] == st:
                        pe.wait_ge(weighed, f * TILES + j + 1)
                        if j == 0 and not first_block:
                            pe.wait_ge(out_ready, KC * f)
                        for m in range(KC):
                            last = nc.tensor.matmul(down_ps[:, m * TOK:(m + 1) * TOK],
                                                    wd[:, j, m * P:(m + 1) * P], hidden[:, j, :],
                                                    start=j == m == 0, stop=j == TILES - 1,
                                                    skip_group_check=True)
                        last.then_inc(down_ready, 1)

            def one_block(b, f, finish):
                for st in range(STAGES):
                    couple(b, st)
                    if f is not None:
                        if isinstance(f, int) and st == 0:
                            pe.wait_ge(in_wd, 2 * 16)
                            pe.wait_ge(setup_v, SETUP_V)
                        ffn(f, st)
                        for _ in range(WARM[st]):
                            nc.tensor.matmul(warm_ps[:, 0:P], c16[:, 0, 0, 0:P], c16[:, 0, 0, 0:P],
                                             start=True, stop=True)

            blocks(pe, one_block)
            for st in range(STAGES):
                ffn(BLOCKS - 1, st)

        @block.vector
        def _(dve):
            done = [0]

            def step(ins):
                done[0] += 1
                ins.then_inc(setup_v, 1)
                dve.wait_ge(setup_v, done[0])

            nc.vector.memset(gate_t[:], 0.0).then_inc(zeroed, 1)
            nc.vector.memset(ones[:], 1.0)
            nc.vector.memset(w3_t[:], W3)
            nc.vector.memset(w1_t[:], W1)
            nc.vector.memset(drive[:, T], 0.0)
            nc.vector.memset(comb3[:], 0.0)
            nc.vector.memset(w16[:, :, :, :, F:FP], 0.0)
            nc.vector.memset(wd[(F % P):P, TILES - 1, :], 0.0)

            def power(n, col, source, axis):
                step(nc.vector.tensor_reduce(most[:, col:col + 1], source, axis, ALU.max,
                                             apply_absolute_value=True))
                dve.wait_ge(setup_t, n + 1)
                step(nc.vector.reduce_max(most1[0:1, col:col + 1], route_ps[0:1, 0:P], AX.X))
                dve.wait_ge(setup_t, n + 2)
                e = ebits[:, col:col + 1]
                step(nc.vector.tensor_copy(most[:, col:col + 1], route_ps[:, 0:1]))
                step(nc.vector.tensor_scalar(e, most[:, col:col + 1].bitcast(U32), 0x7F800000, None,
                                             ALU.bitwise_and))
                step(nc.vector.tensor_scalar(e, e, float(15 << 23), None, ALU.max))
                step(nc.vector.tensor_scalar(scale[:, col:col + 1].bitcast(U32), e, -1.0, float(268 << 23),
                                             ALU.mult, ALU.add))
                step(nc.vector.tensor_scalar(unscale[:, col:col + 1].bitcast(U32), e, float(-(14 << 23)), None,
                                             ALU.add))

            dve.wait_ge(in_core, 5 * 16)
            power(0, 0, cf[:], AX.XY)
            step(nc.vector.tensor_scalar(c16[:, 0], cf[:], scale[:, 0:1], None, ALU.mult))
            step(nc.vector.scalar_tensor_tensor(c16[:, 1], cf[:], scale[:, 0:1], c16[:, 0], ALU.mult,
                                                ALU.subtract))
            dve.wait_ge(in_w, 16)
            w_flat = wf[:].rearrange("p k h f -> p (k h f)")
            power(2, 1, w_flat, AX.X)
            w_hi = w16[:, 0].rearrange("p k h f -> p (k h) f")[:, :, 0:F]
            w_lo = w16[:, 1].rearrange("p k h f -> p (k h) f")[:, :, 0:F]
            w_in = wf[:].rearrange("p k h f -> p (k h) f")
            step(nc.vector.tensor_scalar(w_hi, w_in, scale[:, 1:2], None, ALU.mult))
            step(nc.vector.scalar_tensor_tensor(w_lo, w_in, scale[:, 1:2], w_hi, ALU.mult, ALU.subtract))
            dve.wait_ge(in_const, 5 * 16)
            step(nc.vector.tensor_copy(ident_b[:], ident[:]))
            for k in (0, 2, 3):
                last = nc.vector.tensor_scalar(c_un[:, k:k + 1], unscale[:, 0:1], C[k], None, ALU.mult)
            step(last)
            step(nc.vector.tensor_scalar(p_in[0][:], p_raw[:], SHIFT, None, ALU.subtract))
            assert done[0] == SETUP_V

            def scan_stage(b, st, slots):
                i, k = st // 4, st % 4
                n = b * STAGES + st
                t = b * STEPS + i
                q = q_in[k][:] if k else q0_of(i)
                if k:
                    dve.wait_ge(q_ready, n)
                elif not (isinstance(t, int) and t == 0):
                    dve.wait_ge(q_clipped, t)
                nc.vector.scalar_tensor_tensor(square[:], q, -C[k] / 3.0, q, ALU.mult, ALU.mult
                                               ).then_inc(squared, 1)
                if k:
                    other_part(k, n, t)
                dve.wait_ge(squared, n + 1)
                nc.vector.scalar_tensor_tensor(cubic[:], square[:], C[k], q, ALU.add, ALU.mult
                                               ).then_inc(cubed, 1)
                dve.wait_ge(tanh_ready, n + 1)
                nc.vector.tensor_tensor(th_lo[:], th[:], th_hi[:], ALU.subtract).then_inc(lo_ready, 1)
                if k == 0:
                    other_part(k, n, t)
                if k == 3:
                    dve.wait_ge(rested, t * 5 + 4)
                    nc.vector.scalar_tensor_tensor(rest[:], q, W1, rest4[:], ALU.mult, ALU.add
                                                   ).then_inc(rested, 1)
                slots(0)
                nc.vector.scalar_tensor_tensor(slope[:], p_in[k][:], -BETA, q, ALU.mult, ALU.add
                                               ).then_inc(sloped, 1)
                dve.wait_ge(cubed, n + 1)
                dve.wait_ge(rested, t * 5 + (1, 2, 3, 5)[k])
                nc.vector.tensor_tensor(force[:], cubic[:], rest[:], ALU.add).then_inc(forced, 1)
                slots(1)
                slots(2)
                if k == 2:
                    dve.wait_ge(base_ready, t * BASE + B_DQD)
                    nc.vector.scalar_tensor_tensor(s4[:], q, 2 * W3, dqd[:], ALU.mult, ALU.add
                                                   ).then_inc(s4_ready, 1)
                dve.wait_ge(forced, n + 1)
                dve.wait_ge(coupled, n + 1)
                nc.vector.scalar_tensor_tensor(
                    q_raw[:] if k == 3 else q_in[k + 1][:], coup_ps[:, 0:CB].rearrange("p (m b) -> p m b", m=KC),
                    c_un[:, (0, 0, 2, 3)[k]:(0, 0, 2, 3)[k] + 1], force[:], ALU.mult, ALU.add
                ).then_inc(q_ready, 1)
                dve.wait_ge(sloped, n + 1)
                if k == 3:
                    dve.wait_ge(base_ready, t * BASE + B_PV4)
                nc.vector.scalar_tensor_tensor(p_raw[:] if k == 3 else p_in[k + 1][:], slope[:], A[k],
                                               pv4[:] if k == 3 else p_in[0][:], ALU.mult, ALU.add
                                               ).then_inc(p_ready, 1)
                if k == 3:
                    dve.wait_ge(q_ready, n + 1)
                    nc.vector.tensor_scalar(q_trace[:, :, i, :], q_raw[:], CLAMP, -CLAMP, ALU.min, ALU.max
                                            ).then_inc(q_clipped, 1)
                    dve.wait_ge(p_ready, n + 1)
                    nc.vector.tensor_scalar(p_in[0][:], p_raw[:], CLAMP - SHIFT, -CLAMP - SHIFT,
                                            ALU.min, ALU.max).then_inc(p_clipped, 1)

            def other_part(k, n, t):
                if k:
                    dve.wait_ge(p_ready, n)
                elif not (isinstance(t, int) and t == 0):
                    dve.wait_ge(p_clipped, t)
                if k == 3:
                    dve.wait_ge(s4_ready, t + 1)
                else:
                    dve.wait_ge(base_ready, t * BASE + (B_S2, B_S2, B_S3)[k])
                nc.vector.scalar_tensor_tensor(rest4[:] if k == 3 else rest[:], p_in[k][:], -C[k],
                                               (s2, s2, s3, s4)[k][:], ALU.mult, ALU.add
                                               ).then_inc(rested, 1)

            def route(f, st, slot):
                at = {(1, 0): 0, (1, 1): 1, (1, 2): 2, (3, 1): 3, (4, 1): 4, (5, 0): 5, (7, 1): 6}
                r = at.get((st, slot))
                if r is None:
                    return
                if r:
                    dve.wait_ge(routed, f * ROUTE_OPS + r)
                if r == 0:
                    dve.wait_ge(logits_ready, f + 1)
                    op = nc.vector.tensor_copy(logit[:], route_ps[:, 0:E + 1])
                elif r == 1:
                    op = nc.vector.reduce_max(top[:], logit[:, 0:E], AX.X)
                elif r == 2:
                    op = nc.vector.tensor_scalar(shifted[:], logit[:, 0:E], top[:, 0:1], None, ALU.subtract)
                elif r == 3:
                    dve.wait_ge(exp_ready, f + 1)
                    nc.vector.reduce_sum(total[:], expo[:], AX.X)
                    op = nc.vector.max(best[:], expo[:])
                elif r == 4:
                    nc.vector.reciprocal(share[:], total[:])
                    op = nc.vector.max_index(which[:], best[:], expo[:])
                elif r == 5:
                    op = nc.vector.tensor_copy(which_f[:], which[:, 0:2])
                else:
                    dve.wait_ge(prob_ready, f + 1)
                    for rank, one_hot in enumerate((first, second)):
                        op = nc.vector.tensor_scalar(one_hot[:], iota_s[:], which_f[:, rank:rank + 1],
                                                     prob[:, rank:rank + 1], ALU.is_equal, ALU.mult)
                op.then_inc(routed, 1)

            def finish_chunk(f, m):
                dve.wait_ge(down_ready, TILES * (f + 1))
                if not (isinstance(f, int) and f == 0):
                    dve.wait_ge(stored, 16 * f)
                nc.vector.tensor_tensor(
                    out_s[:, m, :].rearrange("p (t b) -> p t b", t=STEPS),
                    down_ps[:, m * TOK:(m + 1) * TOK].rearrange("p (t b) -> p t b", t=STEPS),
                    xs[:, bass.ts(f, STEPS), m, :], ALU.add).then_inc(out_ready, 1)

            def ffn(f, st, slot):
                route(f, st, slot)
                if slot == 1:
                    for j in range(TILES):
                        if SILU_AT[j] == st:
                            dve.wait_ge(silu_ready, f * TILES + j + 1)
                            if not (isinstance(f, int) and f == 0):
                                dve.wait_ge(down_ready, f * TILES + j - TILES + 1)
                            nc.vector.scalar_tensor_tensor(hidden[:, j, :], act_s[:, j % 4, :], unscale[:, 1:2],
                                                           up_ps[j % 4][:, TOK:2 * TOK], ALU.mult, ALU.mult
                                                           ).then_inc(hidden_ready, 1)

            def one_block(b, f, finish):
                for st in range(STAGES):
                    def slots(slot, st=st):
                        if f is not None:
                            ffn(f, st, slot)
                            if finish and st in FINISH_AT and slot == 1:
                                finish_chunk(f - 1, FINISH_AT.index(st))
                    scan_stage(b, st, slots)

            blocks(dve, one_block)
            for st in range(STAGES):
                for slot in range(3):
                    ffn(BLOCKS - 1, st, slot)
                if st in FINISH_AT:
                    finish_chunk(BLOCKS - 2, FINISH_AT.index(st))
            for m in range(KC):
                finish_chunk(BLOCKS - 1, m)

        @block.gpsimd
        def _(pool):
            pool.wait_ge(setup_v, SETUP_V)
            pool.wait_ge(in_core, 5 * 16)
            pool.wait_ge(setup_a, 3 + 3 * KC)
            nc.gpsimd.tensor_copy(drive_now[:], drive[:, 0]).then_inc(drive_at, 1)
            pool.wait_ge(drive_at, 1)

            def scan_stage(b, st):
                i, k = st // 4, st % 4
                n = b * STAGES + st
                t = b * STEPS + i
                done = t * BASE
                q0, p0 = q0_of(i), p_in[0][:]
                first_step = isinstance(t, int) and t == 0
                add, sub, mul = ALU.add, ALU.subtract, ALU.mult
                if k == 0:
                    if not first_step:
                        pool.wait_ge(q_clipped, t)
                        pool.wait_ge(base_ready, done)
                    nc.gpsimd.tensor_tensor(s2[:], q0, drive_now[:, 0], add).then_inc(base_ready, 1)
                    nc.gpsimd.tensor_tensor(s3[:], q0, drive_now[:, 1], add).then_inc(base_ready, 1)
                elif k == 1:
                    pool.wait_ge(p_ready, n)
                    pool.wait_ge(q_ready, n)
                    nc.gpsimd.tensor_tensor(dp[:], p_in[1][:], p0, sub).then_inc(base_ready, 1)
                    nc.gpsimd.tensor_tensor(dq[:], q_in[1][:], q0, sub).then_inc(base_ready, 1)
                    pool.wait_ge(base_ready, done + B_DQ)
                    nc.gpsimd.tensor_tensor(dq3[:], dq[:], w3_t[:], mul).then_inc(base_ready, 1)
                    pool.wait_ge(base_ready, done + B_DQ3)
                    nc.gpsimd.tensor_tensor(dqd[:], dq3[:], drive_now[:, 2], add).then_inc(base_ready, 1)
                elif k == 2:
                    pool.wait_ge(p_ready, n)
                    pool.wait_ge(base_ready, done + B_DP)
                    nc.gpsimd.tensor_tensor(dp3[:], dp[:], w3_t[:], mul).then_inc(base_ready, 1)
                    nc.gpsimd.tensor_scalar(pw3[:], p_in[2][:], 2 * W3, None, mul).then_inc(base_ready, 1)
                    pool.wait_ge(base_ready, done + B_PW3)
                    nc.gpsimd.tensor_tensor(pv3[:], pw3[:], dp3[:], add).then_inc(base_ready, 1)
                else:
                    pool.wait_ge(p_ready, n)
                    nc.gpsimd.tensor_tensor(pw4[:], p_in[3][:], w1_t[:], mul).then_inc(base_ready, 1)
                    pool.wait_ge(base_ready, done + B_PW4)
                    nc.gpsimd.tensor_tensor(pv4[:], pv3[:], pw4[:], add).then_inc(base_ready, 1)
                    nc.gpsimd.tensor_copy(drive_now[:], drive[:, t + 1]).then_inc(base_ready, 1)

            def ffn(f, st):
                if st == 0:
                    pool.wait_ge(q_split, 2 * f + 1)
                    nc.gpsimd.tensor_tensor(q_lo[:], q_trace[:].rearrange("p m t b -> p m (t b)"), q_hi[:],
                                            ALU.subtract).then_inc(q_split, 1)
                if st == 1:
                    pool.wait_ge(routed, f * ROUTE_OPS + 3)
                    nc.gpsimd.tensor_tensor(expo[:], e_s[:], shifted[:], ALU.pow).then_inc(exp_ready, 1)
                if st == 7:
                    pool.wait_ge(routed, (f + 1) * ROUTE_OPS)
                    pool.wait_ge(gate_ready, f + 1)
                    nc.gpsimd.tensor_tensor(comb[:, 0:E], first[:], second[:], ALU.add).then_inc(parted, 1)
                    nc.gpsimd.tensor_scalar(comb[:, E:E + 1], gate_t[:], 0.5, 0.5, ALU.mult, ALU.add
                                            ).then_inc(parted, 1)
                if st == 8:
                    pool.wait_ge(parted, f * PARTS + 3)
                    nc.gpsimd.tensor_tensor(comb_r[:], comb[:], comb3[:, 0, 0:E + 1], ALU.subtract
                                            ).then_inc(parted, 1)
                if st == 9:
                    pool.wait_ge(parted, f * PARTS + 5)
                    nc.gpsimd.tensor_tensor(comb3[:, 2, 0:E + 1], comb_r[:], comb3[:, 1, 0:E + 1],
                                            ALU.subtract).then_inc(parted, 1)
                for j in range(TILES):
                    if WEIGH_AT[j] == st:
                        pool.wait_ge(hidden_ready, f * TILES + j + 1)
                        pool.wait_ge(comb_copied, f * TILES + j + 1)
                        nc.gpsimd.tensor_tensor(hidden[:, j, :], hidden[:, j, :], comb_s[:, j, :], ALU.mult
                                                ).then_inc(weighed, 1)

            def one_block(b, f, finish):
                for st in range(STAGES):
                    scan_stage(b, st)
                    if f is not None:
                        ffn(f, st)

            blocks(pool, one_block)
            for st in range(STAGES):
                ffn(BLOCKS - 1, st)


def kernel(x, cond_2048, L0_cond_coupling, L0_cond_bias, L0_ffn_W_router, L0_ffn_W_sgate,
           L0_ffn_Ws_gate_up, L0_ffn_Ws_down, L0_ffn_We_gate_up, L0_ffn_We_down):
    import ml_dtypes
    import numpy as np
    import concourse.bacc as bacc
    from concourse.bass_utils import run_bass_kernel_spmd

    def features_first(w):
        w = np.asarray(w)
        return np.ascontiguousarray(w.reshape(KC, P, *w.shape[1:]).swapaxes(0, 1))

    up = np.asarray(L0_ffn_We_gate_up)
    shared = np.asarray(L0_ffn_Ws_gate_up)
    halves = [np.concatenate([up[:, :, h * I_MOE:(h + 1) * I_MOE].transpose(1, 0, 2).reshape(N, E * I_MOE),
                              shared[:, h * I_SH:(h + 1) * I_SH]], axis=1) for h in range(2)]
    down = np.concatenate([np.asarray(L0_ffn_We_down).reshape(E * I_MOE, N), np.asarray(L0_ffn_Ws_down)])
    spread = np.zeros((96, FP), ml_dtypes.bfloat16)
    for part in range(3):
        for e in range(E):
            spread[32 * part + e, e * I_MOE:(e + 1) * I_MOE] = 1
        spread[32 * part + E, E * I_MOE:F] = 1
    arrays = {
        "x": np.ascontiguousarray(np.asarray(x).reshape(B, T, KC, P).transpose(3, 1, 2, 0)),
        "cond": features_first(np.asarray(cond_2048).T),
        "coupling": features_first(np.asarray(L0_cond_coupling).T),
        "bias": features_first(L0_cond_bias),
        "w_up": features_first(np.stack(halves, axis=1)),
        "w_down": down,
        "w_route": features_first(np.concatenate([np.asarray(L0_ffn_W_router), np.asarray(L0_ffn_W_sgate)]).T),
        "identity": np.eye(P, dtype=np.float32),
        "spread": spread,
        "iota": np.tile(np.arange(E, dtype=np.float32), (P, 1)),
        "e_base": np.full((P, E), np.e, np.float32),
    }
    nc = bacc.Bacc("TRN2", target_bir_lowering=False, num_devices=1)
    args = {n: nc.dram_tensor(f"in_{n}", a.shape, mybir.dt.from_np(a.dtype), kind="ExternalInput").ap()
            for n, a in arrays.items()}
    out = nc.dram_tensor("out_0", (P, KC, T * B), F32, kind="ExternalOutput").ap()
    program(nc, **args, out=out)
    r = run_bass_kernel_spmd(nc, [{f"in_{n}": a for n, a in arrays.items()}], core_ids=[0])
    got = r.results[0]["out_0"]
    return np.ascontiguousarray(got.reshape(P, KC, T, B).transpose(3, 2, 1, 0).reshape(B, T, N))
```
